# Optimizing a Trainium2 kernel written in Bass

```python
import numpy as np
import jax
import jax.numpy as jnp

def _softmax(x, axis=-1):
    return jax.nn.softmax(x, axis=axis)

def _gelu(x):
    return jax.nn.gelu(x, approximate=True)

def _silu(x):
    return jax.nn.silu(x)

def _sigmoid(x):
    return jax.nn.sigmoid(x)

def _layernorm(x, axis=-1, eps=1e-05):
    m = jnp.mean(x, axis=axis, keepdims=True)
    v = jnp.var(x, axis=axis, keepdims=True)
    return (x - m) / jnp.sqrt(v + eps)

def _scatter_add(tgt, idx, src, axis=0):
    return tgt.at[idx].add(src)

def _segment_sum(src, seg, n):
    return jax.ops.segment_sum(src, seg, n)
kernel_name = 'mk_adj_resnorm_d1_adj_r2_64b2d9'

def setup_inputs(seed: int=0):
    np.random.seed(seed)
    _w = jnp.asarray

    def _rec_inputs():
        import jax
        import jax.numpy as jnp
        _gk = jax.random.key(seed)
        x = -0.0002928 + 1 * jax.random.normal(jax.random.fold_in(_gk, 1), (8192, 256), jnp.float32)
        _a = jax.random.bernoulli(jax.random.fold_in(_gk, 2), 0.000244141, (8192, 8192))
        _a = jnp.logical_or(_a, jnp.eye(8192, dtype=bool))
        _af = _a.astype(jnp.float32)
        _af = _af * jax.random.uniform(jax.random.fold_in(_gk, 3), (8192, 8192), jnp.float32, 0.05, 1)
        adj = _af
        return (x, adj)
    x, adj = _rec_inputs()

    def _L0_gnn_setup():
        import jax, jax.numpy as jnp
        import numpy as np

        def _bin_sign(v):
            return jnp.sign(v)

        def _bin_sign_z(v):
            return jnp.maximum(jnp.sign(v), 0.0)
        key = jax.random.key(seed)
        k1, k2, k3 = jax.random.split(key, 3)
        N, D_IN, D_OUT = (4096, 256, 256)
        x = jax.random.normal(k1, (N, D_IN), dtype=jnp.float32)
        support = jax.random.uniform(k2, (N, N), dtype=jnp.float32)
        weight = jax.random.normal(k3, (D_OUT, D_IN), dtype=jnp.float32)
        return {'x': x, 'support': support, 'weight': weight}
    _L0_gnn_all = _L0_gnn_setup()
    _L0_gnn_in = {k: v for k, v in _L0_gnn_all.items() if k in ('weight',)}
    del _L0_gnn_all
    return {'x': x, 'adj': adj, 'L0_gnn_weight': _L0_gnn_in['weight']}

def reference(x, adj, L0_gnn_weight):
    import jax
    import jax.numpy as jnp

    def _L0_gnn_ref(x, support, weight):
        import jax, jax.numpy as jnp
        import numpy as np

        def _bin_sign(v):
            return jnp.sign(v)

        def _bin_sign_z(v):
            return jnp.maximum(jnp.sign(v), 0.0)
        bw = _bin_sign(weight)
        ba = _bin_sign_z(x)
        xw = ba @ bw.T
        out = support @ xw
        return jax.nn.relu(out)
    x = _layernorm(x + _L0_gnn_ref(x, adj, L0_gnn_weight), axis=-1)
    return x

_drawn_inputs = setup_inputs


def setup_inputs(seed=0):
    import zlib

    import numpy as np

    out = dict(_drawn_inputs(seed))
    spreads = {}
    factors = {}
    for name, (base, spread) in spreads.items():
        noise = np.random.default_rng([zlib.crc32(name.encode()), seed]).standard_normal(out[name].shape)
        drawn = base * np.exp(spread * noise) if base else spread * noise
        out[name] = jnp.asarray(drawn.astype(out[name].dtype))
    for name, factor in factors.items():
        out[name] = (out[name] * factor).astype(out[name].dtype)
    return out
```

```python
import concourse.bass as bass
from concourse import mybir
from contextlib import ExitStack


P = 128
Q = 32
G = P // Q
BANK = 512


def build(nc, x, adj, w, out):
    f32, f32r, bf16 = mybir.dt.float32, mybir.dt.float32r, mybir.dt.bfloat16
    ALU = mybir.AluOpType
    ACT = mybir.ActivationFunctionType
    N, D = x.shape
    MB = BANK
    NT = MB // Q
    MT = MB // P
    NBLK = N // MB
    PAIRS = NBLK // 2
    DH = D // P
    SLOTS = 2
    CH = 4
    KC = N // CH
    KG = KC // G
    KB = KG // Q
    UK = 2
    UE = UK * MB
    UPC = KB // UK
    UB = CH * UPC
    UP = 2 * UB
    RING = 5
    TP, TV = 3, 2
    EPS = 1e-5
    PGK = 4
    PGROUPS = N // P // PGK
    XQ = KB

    kinds = ("VPP" * UB)[:UB - 2] + "VP"
    kind = [kinds[n % UB] for n in range(UP)]
    before = {k: [kind[:n].count(k) for n in range(UP + 1)] for k in "PV"}
    NP_, NV_ = before["P"][UP], before["V"][UP]
    assert NP_ % TP == 0 and NV_ % TV == 0

    adj_v = adj.rearrange("(q h t i) (c g k) -> q h c g i t k", h=2, t=NT, i=Q, c=CH, g=G)
    x_turn = x.rearrange("(c g b j) d -> c g j b d", c=CH, g=G, b=KB)
    x_rows = x.rearrange("(q h m p) d -> q h p m d", h=2, m=MT, p=P)
    out_rows = out.rearrange("(q h m p) d -> q h p m d", h=2, m=MT, p=P)
    w_rows = w.rearrange("(a p) i -> p a i", p=P)

    ctx = ExitStack()
    with ctx:
        def sb(name, shape, dt):
            return ctx.enter_context(nc.sbuf_tensor(name, shape, dt))

        def sem(name):
            return ctx.enter_context(nc.semaphore(name))

        raw = sb("raw", [P, SLOTS, NT * KG], f32)
        xw = sb("xw", [P, CH * KB, D], f32r)
        turned = sb("turned", [P, TP, UE], f32)
        hi = sb("hi", [P, RING, UE], f32r)
        lo = sb("lo", [P, RING, UE], f32r)
        rows = sb("rows", [P, 2, MT, D], f32)
        relu = sb("relu", [P, DH, MB], f32)
        ident = sb("ident", [P, P], f32)
        ident_b = sb("ident_b", [P, P], bf16)
        stats = sb("stats", [P, MT, 6], f32)
        mv = sb("mv", [P, MT, 2], f32)
        std = sb("std", [P, MT], f32)
        rstd = sb("rstd", [P, MT], f32)
        shift = sb("shift", [P, MT], f32)
        eps = sb("eps", [P, 1], f32)
        step_x = sb("step_x", [P, 2, PGK, D], bf16)
        step_xT = sb("step_xT", [P, 2, PGK, DH, P], bf16)
        w_sb = sb("w_sb", [P, DH, D], f32)
        w_neg = sb("w_neg", [P, DH, D], f32)
        sign_w = sb("sign_w", [P, DH, D], bf16)
        sign_wT = sb("sign_wT", [P, DH, D], bf16)

        ps = ctx.enter_context(nc.psum_tensor("ps", [P, 8 * BANK], f32))
        acc = [[ps[:, (2 * h + a) * BANK:(2 * h + a + 1) * BANK] for a in range(DH)] for h in range(2)]
        back = [ps[:, 2 * h * BANK:2 * (h + 1) * BANK].rearrange("p (m d) -> p m d", m=MT) for h in range(2)]
        turned_v = [ps[:, (4 + 2 * s) * BANK:(6 + 2 * s) * BANK] for s in range(TV)]
        ps_wT = ps[:, 7 * BANK:8 * BANK].bitcast(bf16)[:, 0:DH * D].rearrange("p (a d) -> p a d", a=DH)
        ps_xT = [ps[:, s * BANK:(s + 1) * BANK].bitcast(bf16).rearrange("p (k a n) -> p k a n", k=PGK, a=DH)
                 for s in range(2)]
        ps_xw = [ps[:, (2 + 2 * s) * BANK:(4 + 2 * s) * BANK].rearrange("p (k d) -> p k d", k=PGK)
                 for s in range(2)]

        w_loaded = sem("w_loaded")
        xq_loaded = [sem(f"xq_loaded{c}") for c in range(CH)]
        adj_loaded = [sem(f"adj_loaded{s}") for s in range(SLOTS)]
        rows_loaded = [sem(f"rows_loaded{h}") for h in range(2)]
        rows_stored = [sem(f"rows_stored{h}") for h in range(2)]
        zeroed = sem("zeroed")
        idents_made = sem("idents_made")
        w_negs = sem("w_negs")
        signs_made = sem("signs_made")
        signs_turned = sem("signs_turned")
        signs_copied = sem("signs_copied")
        steps_made = sem("steps_made")
        steps_turned = sem("steps_turned")
        steps_copied = sem("steps_copied")
        xw_made = sem("xw_made")
        xw_copied = sem("xw_copied")
        units_turned = sem("units_turned")
        his_made = sem("his_made")
        p_los_made = sem("p_los_made")
        v_los_made = sem("v_los_made")
        units_used = sem("units_used")
        relus_made = sem("relus_made")
        relus_turned = sem("relus_turned")
        sums_made = sem("sums_made")
        stats_made = sem("stats_made")
        mvs_made = sem("mvs_made")
        stds_made = sem("stds_made")
        rstds_made = sem("rstds_made")
        shifts_made = sem("shifts_made")
        blocks_done = sem("blocks_done")

        block = ctx.enter_context(nc.Block())

        def slot_of(n, count, total):
            s = n % count
            return s, n - count if n >= count else max(m for m in range(total) if m % count == s) - total

        def known_met(value):
            return isinstance(value, int) and value <= 0

        @block.sync
        def _(sp):
            sp.dma_start(w_sb[:], w_rows).then_inc(w_loaded, 16)
            for c in range(CH):
                half = raw[:, c // 2, (c % 2) * XQ * D:(c % 2 + 1) * XQ * D].rearrange("p (b d) -> p b d", d=D)
                for g in range(G):
                    sp.dma_start(half[g * Q:(g + 1) * Q], x_turn[c, g]).then_inc(xq_loaded[c], 16)

            def load_chunk(q, h, c):
                s = c % SLOTS
                n = (q * 2 + h) * CH + c
                if isinstance(n, int) and n < SLOTS:
                    sp.wait_ge(steps_made, (n + 1) * PGROUPS // SLOTS)
                else:
                    sp.wait_ge(units_turned, (n - SLOTS + 1) * UPC)
                dst = raw[:, s, :].rearrange("p (t k) -> p t k", t=NT)
                for g in range(G):
                    sp.dma_start(dst[g * Q:(g + 1) * Q], adj_v[q, h, c, g]).then_inc(adj_loaded[s], 16)

            def store_rows(q, h):
                sp.wait_ge(blocks_done, q * 2 + h + 1)
                sp.dma_start(out_rows[q, h], rows[:, h]).then_inc(rows_stored[h], 16)

            def blocks(q):
                for h in range(2):
                    load_chunk(q, h, 0)
                    if not (isinstance(q, int) and q == 0):
                        store_rows(q - 1, h)
                    load_chunk(q, h, 1)
                    load_chunk(q, h, 2)
                    if not known_met(q):
                        sp.wait_ge(rows_stored[h], q * 16)
                    sp.dma_start(rows[:, h], x_rows[q, h]).then_inc(rows_loaded[h], 16)
                    load_chunk(q, h, 3)

            blocks(0)
            with sp.Fori(1, PAIRS) as q:
                blocks(q)
            for h in range(2):
                store_rows(PAIRS - 1, h)
            for h in range(2):
                sp.wait_ge(rows_stored[h], PAIRS * 16)

        @block.gpsimd
        def _(pool):
            pool.memset(ident[:], 0.0).then_inc(zeroed, 1)
            pool.memset(ident_b[:], 0.0).then_inc(zeroed, 1)
            pool.memset(eps[:], EPS).then_inc(idents_made, 1)
            pool.wait_ge(zeroed, 2)
            for m in (ident, ident_b):
                pool.affine_select(out=m[:], in_=m[:], compare_op=ALU.not_equal, fill=1.0, base=0,
                                   pattern=[[-1, P]], channel_multiplier=1).then_inc(idents_made, 1)

            def pair(q):
                for n in range(UP):
                    if kind[n] != "P":
                        continue
                    t, _ = slot_of(before["P"][n], TP, NP_)
                    s, _ = slot_of(n, RING, UP)
                    pool.wait_ge(his_made, q * UP + n + 1)
                    pool.tensor_tensor(lo[:, s], turned[:, t], hi[:, s].bitcast(f32),
                                       ALU.subtract).then_inc(p_los_made, 1)

            pair(0)
            with pool.Fori(1, PAIRS) as q:
                pair(q)

        @block.scalar
        def _(act):
            for n in range(PGROUPS):
                act.wait_ge(xw_made, n + 1)
                act.activation(xw[:, n * PGK:(n + 1) * PGK], ps_xw[n % 2], ACT.Copy).then_inc(xw_copied, 1)

            def make_hi(q, n):
                s, prev = slot_of(n, RING, UP)
                act.wait_ge(units_turned, q * UP + n + 1)
                if not known_met(q * UP + prev + 1):
                    act.wait_ge(units_used, q * UP + prev + 1)
                src = (turned[:, slot_of(before["P"][n], TP, NP_)[0]] if kind[n] == "P"
                       else turned_v[slot_of(before["V"][n], TV, NV_)[0]])
                act.activation(hi[:, s], src, ACT.Copy).then_inc(his_made, 1)

            def make_relu(q, h):
                b = q * 2 + h
                act.wait_ge(units_used, (b + 1) * UB)
                if not known_met(b):
                    act.wait_ge(relus_turned, b)
                for a in range(DH):
                    act.activation(relu[:, a], acc[h][a], ACT.Relu).then_inc(relus_made, 1)

            def make_std(q, h):
                act.wait_ge(mvs_made, q * 2 + h + 1)
                act.activation(std[:], mv[:, :, 1], ACT.Sqrt, bias=eps[:]).then_inc(stds_made, 1)

            def normalise(q, h, m):
                if m == 0:
                    act.wait_ge(shifts_made, q * 2 + h + 1)
                last = act.activation(rows[:, h, m], rows[:, h, m], ACT.Identity,
                                      bias=shift[:, m:m + 1], scale=rstd[:, m:m + 1])
                if m == MT - 1:
                    last.then_inc(blocks_done, 1)

            def ending(q, h, u):
                if u == RING - 1:
                    make_relu(q, h)
                if u == 18:
                    make_std(q, h)
                if 22 <= u < 22 + MT:
                    normalise(q, h, u - 22)

            def pair(q):
                for n in range(UP):
                    make_hi(q, n)
                    if n < UB and not (isinstance(q, int) and q == 0):
                        ending(q - 1, 1, n)
                    if n >= UB:
                        ending(q, 0, n - UB)

            act.wait_ge(idents_made, 3)
            pair(0)
            with act.Fori(1, PAIRS) as q:
                pair(q)
            for u in range(UB):
                ending(PAIRS - 1, 1, u)

        @block.vector
        def _(dve):
            dve.wait_ge(w_loaded, 16)
            dve.tensor_scalar(w_neg[:], w_sb[:], 0.0, None, ALU.is_lt).then_inc(w_negs, 1)
            dve.wait_ge(w_negs, 1)
            dve.scalar_tensor_tensor(out=sign_w[:], in0=w_sb[:], scalar=0.0, in1=w_neg[:],
                                     op0=ALU.is_gt, op1=ALU.subtract).then_inc(signs_made, 1)

            def make_step(n):
                c, k = n * PGK // XQ, n * PGK % XQ
                src = raw[:, c // 2, ((c % 2) * XQ + k) * D:((c % 2) * XQ + k + PGK) * D]
                dve.wait_ge(xq_loaded[c], G * 16)
                if n >= 2:
                    dve.wait_ge(steps_turned, n - 1)
                dve.tensor_scalar(step_x[:, n % 2], src.rearrange("p (k d) -> p k d", d=D), 0.0, None,
                                  ALU.is_gt).then_inc(steps_made, 1)

            def copy_step(n):
                dve.wait_ge(steps_turned, n + 1)
                if n >= 2:
                    dve.wait_ge(xw_made, n - 1)
                dve.tensor_copy(step_xT[:, n % 2], ps_xT[n % 2]).then_inc(steps_copied, 1)

            make_step(0)
            dve.wait_ge(signs_turned, 1)
            dve.tensor_copy(sign_wT[:], ps_wT).then_inc(signs_copied, 1)
            for n in range(1, PGROUPS):
                make_step(n)
                copy_step(n - 1)
            copy_step(PGROUPS - 1)
            dve.wait_ge(xw_copied, PGROUPS)

            def turn(q, n):
                h, c, u = n // UB, n % UB // UPC, n % UPC
                if u == 0:
                    s = c % SLOTS
                    dve.wait_ge(adj_loaded[s], ((q * 2 + h) * (CH // SLOTS) + c // SLOTS + 1) * G * 16)
                k = before[kind[n]][n]
                if kind[n] == "P":
                    t, prev = slot_of(k, TP, NP_)
                    dst, freed, value = turned[:, t], p_los_made, q * NP_ + prev + 1
                else:
                    t, prev = slot_of(k, TV, NV_)
                    dst, freed, value = turned_v[t], v_los_made, q * NV_ + prev + 1
                if not known_met(value):
                    dve.wait_ge(freed, value)
                src = raw[:, c % SLOTS, :].rearrange("p (t k j) -> p k t j", t=NT, j=Q)[:, u * UK:(u + 1) * UK]
                dve.transpose(dst.rearrange("p (k t j) -> p k t j", k=UK, j=Q), src).then_inc(units_turned, 1)

            def make_lo(q, n):
                s, _ = slot_of(n, RING, UP)
                dve.wait_ge(his_made, q * UP + n + 1)
                dve.tensor_tensor(lo[:, s], turned_v[slot_of(before["V"][n], TV, NV_)[0]],
                                  hi[:, s].bitcast(f32), ALU.subtract).then_inc(v_los_made, 1)

            def add_rows(q, h):
                dve.wait_ge(relus_turned, q * 2 + h + 1)
                dve.wait_ge(rows_loaded[h], (q + 1) * 16)
                dve.tensor_tensor(rows[:, h], back[h], rows[:, h], ALU.add).then_inc(sums_made, 1)

            def make_stats(q, h):
                dve.wait_ge(sums_made, q * 2 + h + 1)
                for m in range(MT):
                    dve.bn_stats(stats[:, m], rows[:, h, m]).then_inc(stats_made, 1)

            def wait_stats(q, h):
                dve.wait_ge(stats_made, (q * 2 + h + 1) * MT)

            def make_mv(q, h):
                for m in range(MT):
                    last = dve.bn_aggr(mv[:, m], stats[:, m])
                last.then_inc(mvs_made, 1)

            def make_rstd(q, h):
                dve.wait_ge(stds_made, q * 2 + h + 1)
                dve.reciprocal(rstd[:], std[:]).then_inc(rstds_made, 1)

            def make_shift(q, h):
                dve.wait_ge(rstds_made, q * 2 + h + 1)
                dve.scalar_tensor_tensor(out=shift[:], in0=mv[:, :, 0], scalar=-1.0, in1=rstd[:],
                                         op0=ALU.mult, op1=ALU.mult).then_inc(shifts_made, 1)

            def ending(q, h, u):
                for at, step in ((13, add_rows), (14, make_stats), (15, wait_stats), (16, make_mv), (20, make_rstd), (21, make_shift)):
                    if u == at:
                        step(q, h)

            def pair(q):
                for n in range(UP):
                    turn(q, n)
                    if n and kind[n - 1] == "V":
                        make_lo(q, n - 1)
                    if n < UB and not (isinstance(q, int) and q == 0):
                        ending(q - 1, 1, n)
                    if n >= UB:
                        ending(q, 0, n - UB)

            assert kind[UP - 1] == "P"
            pair(0)
            with dve.Fori(1, PAIRS) as q:
                pair(q)
            for u in range(UB):
                ending(PAIRS - 1, 1, u)

        @block.tensor
        def _(pe):
            pe.wait_ge(idents_made, 3)
            pe.wait_ge(signs_made, 1)
            for a in range(DH):
                for i in range(DH):
                    last = pe.transpose(ps_wT[:, i, a * P:(a + 1) * P], sign_w[:, a, i * P:(i + 1) * P], ident_b[:])
            last.then_inc(signs_turned, 1)

            def turn_step(n):
                pe.wait_ge(steps_made, n + 1)
                if n >= 2:
                    pe.wait_ge(steps_copied, n - 1)
                for k in range(PGK):
                    for i in range(DH):
                        last = pe.transpose(ps_xT[n % 2][:, k, i], step_x[:, n % 2, k, i * P:(i + 1) * P],
                                            ident_b[:])
                last.then_inc(steps_turned, 1)

            def make_xw(n):
                pe.wait_ge(steps_copied, n + 1)
                if n >= 2:
                    pe.wait_ge(xw_copied, n - 1)
                for k in range(PGK):
                    for i in range(DH):
                        last = pe.matmul(ps_xw[n % 2][:, k], step_xT[:, n % 2, k, i], sign_wT[:, i],
                                         start=(i == 0), stop=(i == DH - 1))
                last.then_inc(xw_made, 1)

            turn_step(0)
            pe.wait_ge(signs_copied, 1)
            for n in range(1, PGROUPS):
                turn_step(n)
                make_xw(n - 1)
            make_xw(PGROUPS - 1)
            pe.wait_ge(xw_copied, PGROUPS)

            def use_unit(q, n):
                h, u = n // UB, n % UB
                s, _ = slot_of(n, RING, UP)
                if u == 0 and not (isinstance(q, int) and q == 0):
                    pe.wait_ge(sums_made, (q - 1) * 2 + h + 1)
                if kind[n] == "P":
                    pe.wait_ge(p_los_made, q * NP_ + before["P"][n] + 1)
                else:
                    pe.wait_ge(v_los_made, q * NV_ + before["V"][n] + 1)
                for k in range(UK):
                    step = u * UK + k
                    for a in range(DH):
                        for part in (hi, lo):
                            last = pe.matmul(acc[h][a], xw[:, step, a * P:(a + 1) * P],
                                             part[:, s, k * MB:(k + 1) * MB],
                                             start=(step == 0 and part is hi),
                                             stop=(step == CH * KB - 1 and part is lo))
                last.then_inc(units_used, 1)

            def turn_back(q, h):
                pe.wait_ge(relus_made, (q * 2 + h + 1) * DH)
                for m in range(MT):
                    for a in range(DH):
                        last = pe.transpose(back[h][:, m, a * P:(a + 1) * P], relu[:, a, m * P:(m + 1) * P],
                                            ident[:])
                last.then_inc(relus_turned, 1)

            BACK_AT = 4

            def pair(q):
                for n in range(UP):
                    use_unit(q, n)
                    if n == BACK_AT and not (isinstance(q, int) and q == 0):
                        turn_back(q - 1, 1)
                    if n == UB + BACK_AT:
                        turn_back(q, 0)

            pair(0)
            with pe.Fori(1, PAIRS) as q:
                pair(q)
            turn_back(PAIRS - 1, 1)


_INS = ['x', 'adj', 'L0_gnn_weight']
_OUTS = [((8192, 256), 'float32')]


def kernel(**inputs):
    import numpy as _np
    import concourse.bacc as _bacc
    from concourse import mybir as _mybir
    from concourse.bass_utils import run_bass_kernel_spmd as _run

    nc = _bacc.Bacc("TRN2", target_bir_lowering=False, num_devices=1)
    arrays, args = {}, []
    for name in _INS:
        a = _np.ascontiguousarray(inputs[name])
        arrays[f"in_{name}_dram"] = a
        args.append(nc.dram_tensor(f"in_{name}_dram", a.shape, _mybir.dt.from_np(a.dtype), kind="ExternalInput").ap())
    for i, (shape, dtype) in enumerate(_OUTS):
        dt = _mybir.dt.from_np(_np.dtype(dtype))
        args.append(nc.dram_tensor(f"out_{i}_dram", shape, dt, kind="ExternalOutput").ap())
    build(nc, *args)
    r = _run(nc, [arrays], core_ids=[0])
    got = tuple(r.results[0][f"out_{i}_dram"] for i in range(len(_OUTS)))
    return got[0]
```

```python
import concourse.bass as bass
from concourse import mybir
from contextlib import ExitStack


P = 128
Q = 32
G = P // Q
BANK = 512


def build(nc, x, adj, w, out):
    f32, f32r, bf16 = mybir.dt.float32, mybir.dt.float32r, mybir.dt.bfloat16
    ALU = mybir.AluOpType
    ACT = mybir.ActivationFunctionType
    N, D = x.shape
    MB = BANK
    NT = MB // Q
    MT = MB // P
    NBLK = N // MB
    PAIRS = NBLK // 2
    DH = D // P
    SLOTS = 2
    CH = 4
    KC = N // CH
    KG = KC // G
    KB = KG // Q
    UK = 2
    UE = UK * MB
    UPC = KB // UK
    UB = CH * UPC
    UP = 2 * UB
    RING = 5
    V_UNITS = 11
    TP = 3
    EPS = 1e-5
    UPP = 2
    PARTS = UB // UPP
    XPARTS = 8
    XK = CH * KB // XPARTS
    GK = 4
    GROUPS = CH * KB // GK
    UPG = GK // UK
    EARLY = 12
    TURNED = UPP
    STEP_BUFS = 3

    def late(g, delay):
        return 4 * (g - EARLY) + delay

    STEP, TURN, COPY, XW, XW_COPY = 2, 2, 8, 6, 11
    assert all(late(g, XW_COPY) < g * UPG for g in range(EARLY, GROUPS))

    PIECES = [(NBLK - 1, range(0, MT // 2)), (NBLK, range(MT // 2, MT))]

    kinds = ["V" if n % UB * V_UNITS % UB < V_UNITS else "P" for n in range(UP)]
    per_pair = {k: kinds.count(k) for k in "PV"}
    assert per_pair["P"] % TP == 0 and "VV" not in "".join(kinds + kinds[:1])

    def known_met(value):
        return isinstance(value, int) and value <= 0

    def in_pair(n):
        return kinds[:n].count(kinds[n])

    def ordinal(q, n):
        return q * per_pair[kinds[n]] + in_pair(n)

    def ring_slot(n):
        s = n % RING
        return s, n - RING if n >= RING else max(m for m in range(UP) if m % RING == s) - UP

    adj_v = adj.rearrange("(q h t i) (c g k) -> q h c g i t k", h=2, t=NT, i=Q, c=CH, g=G)
    x_turn = x.rearrange("(c g b j) d -> c g j b d", c=CH, g=G, b=KB)
    x_rows = x.rearrange("(q h m p) d -> q h p m d", h=2, m=MT, p=P)
    out_rows = out.rearrange("(q h m p) d -> q h p m d", h=2, m=MT, p=P)
    w_rows = w.rearrange("(a p) i -> p a i", p=P)

    ctx = ExitStack()
    with ctx:
        def sb(name, shape, dt):
            return ctx.enter_context(nc.sbuf_tensor(name, shape, dt))

        def sem(name):
            return ctx.enter_context(nc.semaphore(name))

        with nc.sbuf_tensor("x_sb", [P, CH * KB, D], f32) as x_sb:
            pass
        xw = sb("xw", [P, CH * KB, D], f32r)
        raw = sb("raw", [P, SLOTS, NT * KG], f32)
        turned = sb("turned", [P, TP, UE], f32)
        hi = sb("hi", [P, RING, UE], f32r)
        lo = sb("lo", [P, RING, UE], f32r)
        rows = sb("rows", [P, 2, MT, D], f32)
        relu = sb("relu", [P, DH, MB], f32)
        ident = sb("ident", [P, P], f32)
        ident_b = sb("ident_b", [P, P], bf16)
        stats = sb("stats", [P, MT, 6], f32)
        mv = sb("mv", [P, MT, 2], f32)
        std = sb("std", [P, MT], f32)
        rstd = sb("rstd", [P, MT], f32)
        shift = sb("shift", [P, MT], f32)
        eps = sb("eps", [P, 1], f32)
        step_x = sb("step_x", [P, STEP_BUFS, GK, D], bf16)
        step_xT = sb("step_xT", [P, 2, GK, DH, P], bf16)
        w_sb = sb("w_sb", [P, DH, D], f32)
        w_neg = relu[:, :, 0:D]
        sign_w = sb("sign_w", [P, DH, D], bf16)
        sign_wT = sb("sign_wT", [P, DH, D], bf16)

        ps = ctx.enter_context(nc.psum_tensor("ps", [P, 8 * BANK], f32))
        acc = [[ps[:, (2 * h + a) * BANK:(2 * h + a + 1) * BANK] for a in range(DH)] for h in range(2)]
        back = ps[:, 6 * BANK:8 * BANK].rearrange("p (m d) -> p m d", m=MT)
        turned_v = ps[:, 4 * BANK:6 * BANK]
        ps_xw = [ps[:, 2 * b * BANK:2 * (b + 1) * BANK].rearrange("p (k d) -> p k d", k=GK) for b in range(2)]
        xw_buf = [g % 2 if g < EARLY else 1 for g in range(GROUPS)]
        ps_xT = [ps[:, b * BANK:(b + 1) * BANK].bitcast(bf16).rearrange("p (k a n) -> p k a n", k=GK, a=DH)
                 for b in (6, 7)]
        ps_wT = ps[:, 4 * BANK:5 * BANK].bitcast(bf16)[:, 0:DH * D].rearrange("p (a d) -> p a d", a=DH)

        w_loaded = sem("w_loaded")
        x_loaded = [sem(f"x_loaded{i}") for i in range(XPARTS)]
        parts_loaded = [sem(f"parts_loaded{i}") for i in range(PARTS)]
        adj_loaded = [sem(f"adj_loaded{s}") for s in range(SLOTS)]
        rows_loaded = [sem(f"rows_loaded{h}") for h in range(2)]
        rows_stored = [sem(f"rows_stored{h}") for h in range(2)]
        zeroed = sem("zeroed")
        idents_made = sem("idents_made")
        w_negs = sem("w_negs")
        signs_made = sem("signs_made")
        signs_turned = sem("signs_turned")
        signs_copied = sem("signs_copied")
        steps_made = sem("steps_made")
        steps_turned = sem("steps_turned")
        steps_copied = sem("steps_copied")
        xw_made = sem("xw_made")
        xw_copied = sem("xw_copied")
        units_turned = sem("units_turned")
        his_made = sem("his_made")
        p_los_made = sem("p_los_made")
        v_los_made = sem("v_los_made")
        units_used = sem("units_used")
        first_halves = sem("first_halves")
        relus_made = sem("relus_made")
        relus_turned = sem("relus_turned")
        sums_made = sem("sums_made")
        stats_made = sem("stats_made")
        mvs_made = sem("mvs_made")
        stds_made = sem("stds_made")
        rstds_made = sem("rstds_made")
        shifts_made = sem("shifts_made")
        blocks_done = sem("blocks_done")

        block = ctx.enter_context(nc.Block())

        @block.sync
        def _(sp):
            sp.dma_start(w_sb[:], w_rows).then_inc(w_loaded, 16)

            def load_x(i):
                c, k = i * XK // KB, i * XK % KB
                for g in range(G):
                    sp.dma_start(x_sb[g * Q:(g + 1) * Q, i * XK:(i + 1) * XK],
                                 x_turn[c, g, :, k:k + XK]).then_inc(x_loaded[i], 16)

            def load_part(i):
                c, u = i * UPP // UPC, i * UPP % UPC
                k0, k1 = u * UK * Q, (u + UPP) * UK * Q
                dst = raw[:, c % SLOTS, :].rearrange("p (t k) -> p t k", t=NT)
                if c >= SLOTS:
                    sp.wait_ge(units_turned, (c - SLOTS) * UPC + u + UPP)
                for g in range(G):
                    sp.dma_start(dst[g * Q:(g + 1) * Q, :, k0:k1],
                                 adj_v[0, 0, c, g, :, :, k0:k1]).then_inc(parts_loaded[i], 16)

            def load_chunk(q, h, c):
                s = c % SLOTS
                n = (q * 2 + h) * CH + c
                sp.wait_ge(units_turned, (n - SLOTS + 1) * UPC)
                dst = raw[:, s, :].rearrange("p (t k) -> p t k", t=NT)
                for g in range(G):
                    sp.dma_start(dst[g * Q:(g + 1) * Q], adj_v[q, h, c, g]).then_inc(adj_loaded[s], 16)

            def store_rows(q, h):
                sp.wait_ge(blocks_done, q * 2 + h + 1)
                sp.dma_start(out_rows[q, h], rows[:, h]).then_inc(rows_stored[h], 16)

            def load_rows(q, h):
                if not known_met(q):
                    sp.wait_ge(rows_stored[h], q * 16)
                sp.dma_start(rows[:, h], x_rows[q, h]).then_inc(rows_loaded[h], 16)

            def load_block_0():
                early = EARLY * GK // XK
                for i in range(early - 1):
                    load_x(i)
                for i in range(PARTS):
                    for j in range(early, XPARTS):
                        if late(j * XK // GK, STEP) == i * UPP:
                            load_x(j)
                    load_part(i)
                    if i == 0:
                        load_x(early - 1)
                load_rows(0, 0)

            def load_block(q, h):
                for c in range(CH):
                    load_chunk(q, h, c)
                    if c == 0 and not known_met(q):
                        store_rows(q - 1, h)
                    if c == CH - 2:
                        load_rows(q, h)

            load_block_0()
            load_block(0, 1)
            with sp.Fori(1, PAIRS) as q:
                for h in range(2):
                    load_block(q, h)
            store_rows(PAIRS - 1, 0)
            for b, ms in PIECES:
                sp.wait_ge(blocks_done, b + 1)
                sp.dma_start(out_rows[PAIRS - 1, 1, :, ms[0]:ms[-1] + 1],
                             rows[:, 1, ms[0]:ms[-1] + 1]).then_inc(rows_stored[1], 16)
            sp.wait_ge(rows_stored[0], PAIRS * 16)
            sp.wait_ge(rows_stored[1], (PAIRS - 1 + len(PIECES)) * 16)

        @block.gpsimd
        def _(pool):
            pool.memset(ident[:], 0.0).then_inc(zeroed, 1)
            pool.memset(ident_b[:], 0.0).then_inc(zeroed, 1)
            pool.memset(eps[:], EPS).then_inc(idents_made, 1)
            pool.wait_ge(zeroed, 2)
            for m in (ident, ident_b):
                pool.affine_select(out=m[:], in_=m[:], compare_op=ALU.not_equal, fill=1.0, base=0,
                                   pattern=[[-1, P]], channel_multiplier=1).then_inc(idents_made, 1)

            def pair(q):
                for n in range(UP):
                    if kinds[n] != "P":
                        continue
                    t = in_pair(n) % TP
                    s, _ = ring_slot(n)
                    pool.wait_ge(his_made, q * UP + n + 1)
                    pool.tensor_tensor(lo[:, s], turned[:, t], hi[:, s].bitcast(f32),
                                       ALU.subtract).then_inc(p_los_made, 1)

            pair(0)
            with pool.Fori(1, PAIRS) as q:
                pair(q)

        @block.scalar
        def _(act):
            def copy_xw(n):
                act.wait_ge(xw_made, n + 1)
                act.activation(xw[:, n * GK:(n + 1) * GK], ps_xw[xw_buf[n]], ACT.Copy).then_inc(xw_copied, 1)

            def make_hi(q, n):
                s, prev = ring_slot(n)
                act.wait_ge(units_turned, q * UP + n + 1)
                if not known_met(q * UP + prev + 1):
                    act.wait_ge(units_used, q * UP + prev + 1)
                t = in_pair(n)
                src = turned[:, t % TP] if kinds[n] == "P" else turned_v
                act.activation(hi[:, s], src, ACT.Copy).then_inc(his_made, 1)

            def make_relu(q, h):
                b = q * 2 + h
                act.wait_ge(first_halves, b + 1)
                if not known_met(b):
                    act.wait_ge(relus_turned, b * MT)
                for a in range(DH):
                    if a == 1:
                        act.wait_ge(units_used, (b + 1) * UB)
                    act.activation(relu[:, a], acc[h][a], ACT.Relu).then_inc(relus_made, 1)

            def make_std(b, ms):
                act.wait_ge(mvs_made, b + 1)
                act.activation(std[:, ms], mv[:, ms, 1], ACT.Sqrt, bias=eps[:]).then_inc(stds_made, 1)

            def normalise(b, h, m, last):
                act.wait_ge(shifts_made, b + 1)
                done = act.activation(rows[:, h, m], rows[:, h, m], ACT.Identity,
                                      bias=shift[:, m:m + 1], scale=rstd[:, m:m + 1])
                if last:
                    done.then_inc(blocks_done, 1)

            def ending(q, h, u):
                if u == RING - 1:
                    make_relu(q, h)
                if u == 18:
                    make_std(q * 2 + h, slice(0, MT))
                if 22 <= u < 22 + MT:
                    normalise(q * 2 + h, h, u - 22, u - 22 == MT - 1)

            def pair(q):
                for n in range(UP):
                    if not (known_met(q) and n < TURNED):
                        make_hi(q, n)
                    for g in range(EARLY, GROUPS):
                        if known_met(q) and n == late(g, XW_COPY):
                            copy_xw(g)
                    if n < UB and not known_met(q):
                        ending(q - 1, 1, n)
                    if n >= UB:
                        ending(q, 0, n - UB)

            act.wait_ge(idents_made, 3)
            for g in range(EARLY - XK // GK):
                copy_xw(g)
            for n in range(TURNED):
                make_hi(0, n)
            for g in range(EARLY - XK // GK, EARLY):
                copy_xw(g)
            pair(0)
            with act.Fori(1, PAIRS) as q:
                pair(q)
            make_relu(PAIRS - 1, 1)
            for b, ms in PIECES:
                make_std(b, slice(ms[0], ms[-1] + 1))
                for m in ms:
                    normalise(b, 1, m, m == ms[-1])

        @block.vector
        def _(dve):
            dve.wait_ge(w_loaded, 16)
            dve.tensor_scalar(w_neg, w_sb[:], 0.0, None, ALU.is_lt).then_inc(w_negs, 1)
            dve.wait_ge(w_negs, 1)
            dve.scalar_tensor_tensor(out=sign_w[:], in0=w_sb[:], scalar=0.0, in1=w_neg,
                                     op0=ALU.is_gt, op1=ALU.subtract).then_inc(signs_made, 1)

            def make_step(n):
                dve.wait_ge(x_loaded[n * GK // XK], G * 16)
                if n >= STEP_BUFS:
                    dve.wait_ge(steps_turned, n - STEP_BUFS + 1)
                dve.tensor_scalar(step_x[:, n % STEP_BUFS], x_sb[:, n * GK:(n + 1) * GK], 0.0, None,
                                  ALU.is_gt).then_inc(steps_made, 1)

            def copy_step(n):
                dve.wait_ge(steps_turned, n + 1)
                if n >= 2:
                    dve.wait_ge(xw_made, n - 1)
                dve.tensor_copy(step_xT[:, n % 2], ps_xT[n % 2]).then_inc(steps_copied, 1)

            dve.wait_ge(signs_turned, 1)
            dve.tensor_copy(sign_wT[:], ps_wT).then_inc(signs_copied, 1)

            def turn(q, n):
                h, c, u = n // UB, n % UB // UPC, n % UPC
                s = c % SLOTS
                if known_met(q) and n < UB:
                    if n % UPP == 0:
                        dve.wait_ge(parts_loaded[n // UPP], G * 16)
                elif u == 0:
                    dve.wait_ge(adj_loaded[s], ((q * 2 + h - 1) * (CH // SLOTS) + c // SLOTS + 1) * G * 16)
                t = in_pair(n)
                if known_met(q) and n == 0:
                    dve.wait_ge(signs_copied, 1)
                if kinds[n] == "P":
                    dst = turned[:, t % TP]
                    if not known_met(ordinal(q, n) - TP + 1):
                        dve.wait_ge(p_los_made, ordinal(q, n) - TP + 1)
                else:
                    dst = turned_v
                    if not known_met(ordinal(q, n)):
                        dve.wait_ge(v_los_made, ordinal(q, n))
                src = raw[:, c % SLOTS, :].rearrange("p (t k j) -> p k t j", t=NT, j=Q)[:, u * UK:(u + 1) * UK]
                dve.transpose(dst.rearrange("p (k t j) -> p k t j", k=UK, j=Q), src).then_inc(units_turned, 1)

            def make_lo(q, n):
                s, _ = ring_slot(n)
                dve.wait_ge(his_made, q * UP + n + 1)
                dve.tensor_tensor(lo[:, s], turned_v[:, :],
                                  hi[:, s].bitcast(f32), ALU.subtract).then_inc(v_los_made, 1)

            def add_rows(b, h, ms):
                dve.tensor_tensor(rows[:, h, ms], back[:, ms], rows[:, h, ms], ALU.add).then_inc(sums_made, 1)

            def make_stats(b, h, m):
                dve.wait_ge(sums_made, b + 1)
                dve.bn_stats(stats[:, m], rows[:, h, m]).then_inc(stats_made, 1)

            def make_mv(m):
                return dve.bn_aggr(mv[:, m], stats[:, m])

            def make_rstd(b, ms):
                dve.wait_ge(stds_made, b + 1)
                dve.reciprocal(rstd[:, ms], std[:, ms]).then_inc(rstds_made, 1)

            def make_shift(b, ms):
                dve.wait_ge(rstds_made, b + 1)
                dve.scalar_tensor_tensor(out=shift[:, ms], in0=mv[:, ms, 0], scalar=-1.0, in1=rstd[:, ms],
                                         op0=ALU.mult, op1=ALU.mult).then_inc(shifts_made, 1)

            def ending(q, h, u):
                b, whole = q * 2 + h, slice(0, MT)
                if u == 13:
                    dve.wait_ge(relus_turned, (b + 1) * MT)
                    dve.wait_ge(rows_loaded[h], (q + 1) * 16)
                    add_rows(b, h, whole)
                if u == 14:
                    for m in range(MT):
                        make_stats(b, h, m)
                if u == 15:
                    dve.wait_ge(stats_made, (b + 1) * MT)
                if u == 16:
                    for m in range(MT):
                        last = make_mv(m)
                    last.then_inc(mvs_made, 1)
                if u == 20:
                    make_rstd(b, whole)
                if u == 21:
                    make_shift(b, whole)

            def pair(q):
                for n in range(UP):
                    for g in range(EARLY, GROUPS):
                        if known_met(q) and n == late(g, STEP):
                            make_step(g)
                        if known_met(q) and n == late(g, COPY):
                            copy_step(g)
                    if not (known_met(q) and n < TURNED):
                        turn(q, n)
                    if n and kinds[n - 1] == "V" and not (known_met(q) and n < TURNED):
                        make_lo(q, n - 1)
                    if n < UB and not known_met(q):
                        ending(q - 1, 1, n)
                    if n >= UB:
                        ending(q, 0, n - UB)

            make_step(0)
            for g in range(1, EARLY):
                if g == EARLY - XK // GK:
                    copy_step(g - 1)
                    for n in range(TURNED):
                        turn(0, n)
                    for n in range(TURNED - 1):
                        if kinds[n] == "V":
                            make_lo(0, n)
                make_step(g)
                if g != EARLY - XK // GK:
                    copy_step(g - 1)
            copy_step(EARLY - 1)
            assert kinds[-1] == "P"
            pair(0)
            with dve.Fori(1, PAIRS) as q:
                pair(q)
            dve.wait_ge(rows_loaded[1], PAIRS * 16)
            for b, ms in PIECES:
                dve.wait_ge(relus_turned, (NBLK - 1) * MT + ms[-1] + 1)
                add_rows(b, 1, slice(ms[0], ms[-1] + 1))
                for m in ms:
                    make_stats(b, 1, m)
                dve.wait_ge(stats_made, (NBLK - 1) * MT + ms[-1] + 1)
                for m in ms:
                    last = make_mv(m)
                last.then_inc(mvs_made, 1)
                if b == PIECES[-1][0]:
                    for piece, ps_ in PIECES:
                        make_rstd(piece, slice(ps_[0], ps_[-1] + 1))
                        make_shift(piece, slice(ps_[0], ps_[-1] + 1))

        @block.tensor
        def _(pe):
            pe.wait_ge(idents_made, 3)
            pe.wait_ge(signs_made, 1)
            for a in range(DH):
                for i in range(DH):
                    last = pe.transpose(ps_wT[:, i, a * P:(a + 1) * P], sign_w[:, a, i * P:(i + 1) * P], ident_b[:])
            last.then_inc(signs_turned, 1)

            def turn_step(n):
                pe.wait_ge(steps_made, n + 1)
                if n >= 2:
                    pe.wait_ge(steps_copied, n - 1)
                for k in range(GK):
                    for i in range(DH):
                        last = pe.transpose(ps_xT[n % 2][:, k, i], step_x[:, n % STEP_BUFS, k, i * P:(i + 1) * P],
                                            ident_b[:])
                last.then_inc(steps_turned, 1)

            def make_xw(n):
                pe.wait_ge(steps_copied, n + 1)
                if n >= 2:
                    pe.wait_ge(xw_copied, max(m for m in range(n) if xw_buf[m] == xw_buf[n]) + 1)
                for k in range(GK):
                    for i in range(DH):
                        last = pe.matmul(ps_xw[xw_buf[n]][:, k], step_xT[:, n % 2, k, i], sign_wT[:, i],
                                         start=(i == 0), stop=(i == DH - 1))
                last.then_inc(xw_made, 1)

            turn_step(0)
            pe.wait_ge(signs_copied, 1)
            for g in range(1, EARLY):
                if g == EARLY - XK // GK:
                    make_xw(g - 1)
                turn_step(g)
                if g != EARLY - XK // GK:
                    make_xw(g - 1)
            make_xw(EARLY - 1)

            def use_unit(q, n):
                h, u = n // UB, n % UB
                s, _ = ring_slot(n)
                if known_met(q) and n == 0:
                    pe.wait_ge(xw_copied, EARLY)
                if known_met(q) and n < UB and n % UPG == 0 and n // UPG >= EARLY:
                    pe.wait_ge(xw_copied, n // UPG + 1)
                if u == 0 and not known_met(q):
                    pe.wait_ge(relus_made, ((q - 1) * 2 + h + 1) * DH)
                pe.wait_ge(p_los_made if kinds[n] == "P" else v_los_made, ordinal(q, n) + 1)

                def product(k, a, part):
                    step = u * UK + k
                    return pe.matmul(acc[h][a], xw[:, step, a * P:(a + 1) * P], part[:, s, k * MB:(k + 1) * MB],
                                     start=(step == 0 and part is hi), stop=(step == CH * KB - 1 and part is lo))

                if u == UB - 1:
                    for a in range(DH):
                        for k in range(UK):
                            for part in (hi, lo):
                                last = product(k, a, part)
                        if a == 0:
                            last.then_inc(first_halves, 1)
                else:
                    for k in range(UK):
                        for a in range(DH):
                            for part in (hi, lo):
                                last = product(k, a, part)
                last.then_inc(units_used, 1)

            def turn_back(q, h):
                if not known_met(q * 2 + h):
                    pe.wait_ge(sums_made, q * 2 + h)
                for a in range(DH):
                    pe.wait_ge(relus_made, (q * 2 + h) * DH + a + 1)
                    for m in range(MT):
                        last = pe.transpose(back[:, m, a * P:(a + 1) * P], relu[:, a, m * P:(m + 1) * P],
                                            ident[:])
                        if a == DH - 1:
                            last.then_inc(relus_turned, 1)

            BACK_AT = 4

            def pair(q):
                for n in range(UP):
                    for g in range(EARLY, GROUPS):
                        if known_met(q) and n == late(g, TURN):
                            turn_step(g)
                        if known_met(q) and n == late(g, XW):
                            make_xw(g)
                    use_unit(q, n)
                    if n == BACK_AT and not known_met(q):
                        turn_back(q - 1, 1)
                    if n == UB + BACK_AT:
                        turn_back(q, 0)

            pair(0)
            with pe.Fori(1, PAIRS) as q:
                pair(q)
            turn_back(PAIRS - 1, 1)


_INS = ['x', 'adj', 'L0_gnn_weight']
_OUTS = [((8192, 256), 'float32')]


def kernel(**inputs):
    import numpy as _np
    import concourse.bacc as _bacc
    from concourse import mybir as _mybir
    from concourse.bass_utils import run_bass_kernel_spmd as _run

    nc = _bacc.Bacc("TRN2", target_bir_lowering=False, num_devices=1)
    arrays, args = {}, []
    for name in _INS:
        a = _np.ascontiguousarray(inputs[name])
        arrays[f"in_{name}_dram"] = a
        args.append(nc.dram_tensor(f"in_{name}_dram", a.shape, _mybir.dt.from_np(a.dtype), kind="ExternalInput").ap())
    for i, (shape, dtype) in enumerate(_OUTS):
        dt = _mybir.dt.from_np(_np.dtype(dtype))
        args.append(nc.dram_tensor(f"out_{i}_dram", shape, dt, kind="ExternalOutput").ap())
    build(nc, *args)
    r = _run(nc, [arrays], core_ids=[0])
    got = tuple(r.results[0][f"out_{i}_dram"] for i in range(len(_OUTS)))
    return got[0]
```

```python
import concourse.bass as bass
from concourse import mybir
from contextlib import ExitStack


P = 128
Q = 32
G = P // Q
BANK = 512


def build(nc, x, adj, w, out):
    f32, f32r, bf16 = mybir.dt.float32, mybir.dt.float32r, mybir.dt.bfloat16
    ALU = mybir.AluOpType
    ACT = mybir.ActivationFunctionType
    N, D = x.shape
    MB = BANK
    NT = MB // Q
    MT = MB // P
    NBLK = N // MB
    PAIRS = NBLK // 2
    DH = D // P
    SLOTS = 4
    CH = 8
    KC = N // CH
    KG = KC // G
    KB = KG // Q
    UK = 2
    UE = UK * MB
    UPC = KB // UK
    UB = CH * UPC
    UP = 2 * UB
    RING = 6
    V_UNITS = 10
    TP = 4
    EPS = 1e-5
    UPP = 2
    PARTS = UB // UPP
    XPARTS = 8
    XK = CH * KB // XPARTS
    GK = 4
    GROUPS = CH * KB // GK
    UPG = GK // UK
    EARLY = 10
    TURNED = UPP
    STEP_BUFS = 2

    def late(g, delay):
        return 3 * (g - EARLY) + delay

    STEP, TURN, COPY, XW, XW_COPY = 2, 2, 5, 4, 9
    assert all(late(g, XW_COPY) < g * UPG for g in range(EARLY, GROUPS))

    PIECES = [(NBLK - 1, range(0, MT // 2)), (NBLK, range(MT // 2, MT))]

    kinds = ["V" if n % UB * V_UNITS % UB < V_UNITS else "P" for n in range(UP)]
    per_pair = {k: kinds.count(k) for k in "PV"}
    assert per_pair["P"] % TP == 0 and "VV" not in "".join(kinds + kinds[:1])

    def known_met(value):
        return isinstance(value, int) and value <= 0

    def in_pair(n):
        return kinds[:n].count(kinds[n])

    def ordinal(q, n):
        return q * per_pair[kinds[n]] + in_pair(n)

    def ring_slot(n):
        s = n % RING
        return s, n - RING if n >= RING else max(m for m in range(UP) if m % RING == s) - UP

    adj_v = adj.rearrange("(q h t i) (c g k) -> q h c g i t k", h=2, t=NT, i=Q, c=CH, g=G)
    x_turn = x.rearrange("(c g b j) d -> c g j b d", c=CH, g=G, b=KB)
    x_rows = x.rearrange("(q h m p) d -> q h p m d", h=2, m=MT, p=P)
    out_rows = out.rearrange("(q h m p) d -> q h p m d", h=2, m=MT, p=P)
    w_rows = w.rearrange("(a p) i -> p a i", p=P)

    ctx = ExitStack()
    with ctx:
        def sb(name, shape, dt):
            return ctx.enter_context(nc.sbuf_tensor(name, shape, dt))

        def sem(name):
            return ctx.enter_context(nc.semaphore(name))

        with nc.sbuf_tensor("x_sb", [P, CH * KB, D], f32) as x_sb:
            pass
        xw = sb("xw", [P, CH * KB, D], f32r)
        raw = sb("raw", [P, SLOTS, NT * KG], f32)
        turned = sb("turned", [P, TP, UE], f32)
        hi = sb("hi", [P, RING, UE], f32r)
        lo = sb("lo", [P, RING, UE], f32r)
        rows = sb("rows", [P, MT, D], f32)
        relu = sb("relu", [P, DH, MB], f32)
        ident = sb("ident", [P, P], f32)
        ident_b = sb("ident_b", [P, P], bf16)
        stats = sb("stats", [P, MT, 6], f32)
        mv = sb("mv", [P, MT, 2], f32)
        std = sb("std", [P, MT], f32)
        rstd = sb("rstd", [P, MT], f32)
        shift = sb("shift", [P, MT], f32)
        eps = sb("eps", [P, 1], f32)
        flat = [t.rearrange("p a b -> p (a b)") for t in (relu[:], rows[:])]
        step_x = flat[0].bitcast(bf16).rearrange("p (s k d) -> p s k d", s=STEP_BUFS, k=GK)
        step_xT = flat[1].bitcast(bf16).rearrange("p (s k a n) -> p s k a n", s=2, k=GK, a=DH)
        w_sb, w_neg = (flat[1][:, i * DH * D:(i + 1) * DH * D].rearrange("p (a i) -> p a i", a=DH) for i in range(2))
        sign_w = sb("sign_w", [P, DH, D], bf16)
        sign_wT = sb("sign_wT", [P, DH, D], bf16)

        ps = ctx.enter_context(nc.psum_tensor("ps", [P, 8 * BANK], f32))
        acc = [[ps[:, (2 * h + a) * BANK:(2 * h + a + 1) * BANK] for a in range(DH)] for h in range(2)]
        back = ps[:, 6 * BANK:8 * BANK].rearrange("p (m d) -> p m d", m=MT)
        turned_v = ps[:, 4 * BANK:6 * BANK]
        ps_xw = [ps[:, 2 * b * BANK:2 * (b + 1) * BANK].rearrange("p (k d) -> p k d", k=GK) for b in range(2)]
        xw_buf = [g % 2 if g < EARLY else 1 for g in range(GROUPS)]
        ps_xT = [ps[:, b * BANK:(b + 1) * BANK].bitcast(bf16).rearrange("p (k a n) -> p k a n", k=GK, a=DH)
                 for b in (6, 7)]
        ps_wT = ps[:, 4 * BANK:5 * BANK].bitcast(bf16)[:, 0:DH * D].rearrange("p (a d) -> p a d", a=DH)

        w_loaded = sem("w_loaded")
        x_loaded = [sem(f"x_loaded{i}") for i in range(XPARTS)]
        parts_loaded = [sem(f"parts_loaded{i}") for i in range(PARTS)]
        adj_loaded = [sem(f"adj_loaded{s}") for s in range(SLOTS)]
        rows_loaded = sem("rows_loaded")
        rows_stored = sem("rows_stored")
        zeroed = sem("zeroed")
        idents_made = sem("idents_made")
        w_negs = sem("w_negs")
        signs_made = sem("signs_made")
        signs_turned = sem("signs_turned")
        signs_copied = sem("signs_copied")
        steps_made = sem("steps_made")
        steps_turned = sem("steps_turned")
        early_steps_copied = sem("early_steps_copied")
        late_steps_copied = sem("late_steps_copied")
        xw_made = sem("xw_made")
        xw_copied = sem("xw_copied")
        units_turned = sem("units_turned")
        his_made = sem("his_made")
        p_los_made = sem("p_los_made")
        v_los_made = sem("v_los_made")
        units_used = sem("units_used")
        first_halves = sem("first_halves")
        relus_made = sem("relus_made")
        relus_turned = sem("relus_turned")
        sums_made = sem("sums_made")
        stats_made = sem("stats_made")
        mvs_made = sem("mvs_made")
        stds_made = sem("stds_made")
        rstds_made = sem("rstds_made")
        shifts_made = sem("shifts_made")
        blocks_done = sem("blocks_done")
        last_piece_done = sem("last_piece_done")

        block = ctx.enter_context(nc.Block())

        LOWER, UPPER = range(0, G // 2), range(G // 2, G)
        IN_TURNS = [g for both in zip(LOWER, UPPER) for g in both]

        def start_chunk(eng, q, h, c, quadrants):
            dst = raw[:, c % SLOTS, :].rearrange("p (t k) -> p t k", t=NT)
            for g in quadrants:
                eng.dma_start(dst[g * Q:(g + 1) * Q], adj_v[q, h, c, g]).then_inc(adj_loaded[c % SLOTS], 16)

        @block.sync
        def _(sp):
            sp.dma_start(w_sb, w_rows).then_inc(w_loaded, 16)

            def load_x(i):
                c, k = i * XK // KB, i * XK % KB
                for g in IN_TURNS:
                    sp.dma_start(x_sb[g * Q:(g + 1) * Q, i * XK:(i + 1) * XK],
                                 x_turn[c, g, :, k:k + XK]).then_inc(x_loaded[i], 16)

            def load_part(i):
                c, u = i * UPP // UPC, i * UPP % UPC
                k0, k1 = u * UK * Q, (u + UPP) * UK * Q
                dst = raw[:, c % SLOTS, :].rearrange("p (t k) -> p t k", t=NT)
                if c >= SLOTS:
                    sp.wait_ge(units_turned, (c - SLOTS) * UPC + u + UPP)
                for g in IN_TURNS:
                    sp.dma_start(dst[g * Q:(g + 1) * Q, :, k0:k1],
                                 adj_v[0, 0, c, g, :, :, k0:k1]).then_inc(parts_loaded[i], 16)

            def load_chunk(q, h, c):
                n = (q * 2 + h) * CH + c
                sp.wait_ge(units_turned, (n - SLOTS + 1) * UPC)
                start_chunk(sp, q, h, c, LOWER)

            def block_before(q, h):
                return (q, 0) if h else (q - 1, 1)

            def store_rows(q, h):
                sp.wait_ge(blocks_done, q * 2 + h + 1)
                sp.dma_start(out_rows[q, h], rows[:]).then_inc(rows_stored, 16)

            def load_rows(q, h):
                b = q * 2 + h
                if known_met(b):
                    sp.wait_ge(xw_made, GROUPS)
                else:
                    sp.wait_ge(rows_stored, b * 16)
                sp.dma_start(rows[:], x_rows[q, h]).then_inc(rows_loaded, 16)

            def load_block_0():
                early = EARLY * GK // XK
                for i in range(early - 1):
                    load_x(i)
                for i in range(PARTS):
                    for j in range(early, XPARTS):
                        if late(j * XK // GK, STEP) == i * UPP:
                            load_x(j)
                    load_part(i)
                    if i == 0:
                        load_x(early - 1)

            def load_block(q, h):
                for c in range(CH):
                    load_chunk(q, h, c)
                    if c == 2 and not known_met(q * 2 + h - 1):
                        store_rows(*block_before(*block_before(q, h)))
                    if c == 3:
                        load_rows(*block_before(q, h))

            load_block_0()
            load_block(0, 1)
            with sp.Fori(1, PAIRS) as q:
                for h in range(2):
                    load_block(q, h)
            store_rows(PAIRS - 1, 0)
            load_rows(PAIRS - 1, 1)
            for b, ms in PIECES:
                if b == NBLK - 1:
                    sp.wait_ge(blocks_done, NBLK)
                else:
                    sp.wait_ge(last_piece_done, 1)
                sp.dma_start(out_rows[PAIRS - 1, 1, :, ms[0]:ms[-1] + 1],
                             rows[:, ms[0]:ms[-1] + 1]).then_inc(rows_stored, 16)
            sp.wait_ge(rows_stored, (NBLK - 1 + len(PIECES)) * 16)

        @block.gpsimd
        def _(pool):
            pool.memset(ident[:], 0.0).then_inc(zeroed, 1)
            pool.memset(ident_b[:], 0.0).then_inc(zeroed, 1)
            pool.memset(eps[:], EPS).then_inc(idents_made, 1)
            pool.wait_ge(zeroed, 2)
            for m in (ident, ident_b):
                pool.affine_select(out=m[:], in_=m[:], compare_op=ALU.not_equal, fill=1.0, base=0,
                                   pattern=[[-1, P]], channel_multiplier=1).then_inc(idents_made, 1)

            def pair(q):
                for n in range(UP):
                    if kinds[n] != "P":
                        continue
                    t = in_pair(n) % TP
                    s, _ = ring_slot(n)
                    pool.wait_ge(his_made, q * UP + n + 1)
                    pool.tensor_tensor(lo[:, s], turned[:, t], hi[:, s].bitcast(f32),
                                       ALU.subtract).then_inc(p_los_made, 1)

            pair(0)
            with pool.Fori(1, PAIRS) as q:
                pair(q)

        @block.scalar
        def _(act):
            def copy_late_step(n):
                act.wait_ge(steps_turned, n + 1)
                act.wait_ge(xw_made, n - 1)
                act.activation(step_xT[:, n % 2], ps_xT[n % 2], ACT.Copy).then_inc(late_steps_copied, 1)

            def copy_xw(n):
                act.wait_ge(xw_made, n + 1)
                act.activation(xw[:, n * GK:(n + 1) * GK], ps_xw[xw_buf[n]], ACT.Copy).then_inc(xw_copied, 1)

            def make_hi(q, n):
                s, prev = ring_slot(n)
                act.wait_ge(units_turned, q * UP + n + 1)
                if not known_met(q * UP + prev + 1):
                    act.wait_ge(units_used, q * UP + prev + 1)
                t = in_pair(n)
                src = turned[:, t % TP] if kinds[n] == "P" else turned_v
                act.activation(hi[:, s], src, ACT.Copy).then_inc(his_made, 1)

            def make_relu(q, h):
                b = q * 2 + h
                act.wait_ge(first_halves, b + 1)
                if not known_met(b):
                    act.wait_ge(relus_turned, b * MT)
                for a in range(DH):
                    if a == 1:
                        act.wait_ge(units_used, (b + 1) * UB)
                    act.activation(relu[:, a], acc[h][a], ACT.Relu).then_inc(relus_made, 1)

            def make_std(b, ms):
                act.wait_ge(mvs_made, b + 1)
                act.activation(std[:, ms], mv[:, ms, 1], ACT.Sqrt, bias=eps[:]).then_inc(stds_made, 1)

            def normalise(b, m, last):
                act.wait_ge(shifts_made, b + 1)
                done = act.activation(rows[:, m], rows[:, m], ACT.Identity,
                                      bias=shift[:, m:m + 1], scale=rstd[:, m:m + 1])
                if last:
                    done.then_inc(blocks_done, 1)

            def ending(q, h, u):
                if u == RING - 1:
                    make_relu(q, h)
                if u == 18:
                    make_std(q * 2 + h, slice(0, MT))
                if 22 <= u < 22 + MT:
                    normalise(q * 2 + h, u - 22, u - 22 == MT - 1)

            def load_chunk_after(q, n):
                later, c = divmod(n // UPC + SLOTS, 2 * CH)
                in_block_0 = known_met(q) and n // UPC + SLOTS < CH
                beyond_the_end = isinstance(q, int) and q + later >= PAIRS
                if n % UPC == UPC - 1 and not in_block_0 and not beyond_the_end:
                    start_chunk(act, q + later, c // CH, c % CH, UPPER)

            def pair(q):
                for n in range(UP):
                    if not (known_met(q) and n < TURNED):
                        make_hi(q, n)
                        load_chunk_after(q, n)
                    for g in range(EARLY, GROUPS):
                        if known_met(q) and n == late(g, COPY):
                            copy_late_step(g)
                        if known_met(q) and n == late(g, XW_COPY):
                            copy_xw(g)
                    if n < UB and not known_met(q):
                        ending(q - 1, 1, n)
                    if n >= UB:
                        ending(q, 0, n - UB)

            act.wait_ge(idents_made, 3)
            for g in range(EARLY - XK // GK):
                copy_xw(g)
            for n in range(TURNED):
                make_hi(0, n)
            for g in range(EARLY - XK // GK, EARLY):
                copy_xw(g)
            pair(0)
            with act.Fori(1, PAIRS - 1) as q:
                pair(q)
            pair(PAIRS - 1)
            make_relu(PAIRS - 1, 1)
            for b, ms in PIECES:
                make_std(b, slice(ms[0], ms[-1] + 1))
            b, ms = PIECES[0]
            for m in ms:
                normalise(b, m, m == ms[-1])

        @block.vector
        def _(dve):
            dve.wait_ge(w_loaded, 16)
            dve.tensor_scalar(w_neg, w_sb, 0.0, None, ALU.is_lt).then_inc(w_negs, 1)
            dve.wait_ge(w_negs, 1)
            dve.scalar_tensor_tensor(out=sign_w[:], in0=w_sb, scalar=0.0, in1=w_neg,
                                     op0=ALU.is_gt, op1=ALU.subtract).then_inc(signs_made, 1)

            def make_step(n):
                dve.wait_ge(x_loaded[n * GK // XK], G * 16)
                if n >= STEP_BUFS:
                    dve.wait_ge(steps_turned, n - STEP_BUFS + 1)
                dve.tensor_scalar(step_x[:, n % STEP_BUFS], x_sb[:, n * GK:(n + 1) * GK], 0.0, None,
                                  ALU.is_gt).then_inc(steps_made, 1)

            def copy_early_step(n):
                dve.wait_ge(steps_turned, n + 1)
                if n >= 2:
                    dve.wait_ge(xw_made, n - 1)
                dve.tensor_copy(step_xT[:, n % 2], ps_xT[n % 2]).then_inc(early_steps_copied, 1)

            dve.wait_ge(signs_turned, 1)
            dve.tensor_copy(sign_wT[:], ps_wT).then_inc(signs_copied, 1)

            def turn(q, n):
                h, c, u = n // UB, n % UB // UPC, n % UPC
                s = c % SLOTS
                if known_met(q) and n < UB:
                    if n % UPP == 0:
                        dve.wait_ge(parts_loaded[n // UPP], G * 16)
                elif u == 0:
                    dve.wait_ge(adj_loaded[s], ((q * 2 + h - 1) * (CH // SLOTS) + c // SLOTS + 1) * G * 16)
                t = in_pair(n)
                if known_met(q) and n == 0:
                    dve.wait_ge(signs_copied, 1)
                if kinds[n] == "P":
                    dst = turned[:, t % TP]
                    if not known_met(ordinal(q, n) - TP + 1):
                        dve.wait_ge(p_los_made, ordinal(q, n) - TP + 1)
                else:
                    dst = turned_v
                    if not known_met(ordinal(q, n)):
                        dve.wait_ge(v_los_made, ordinal(q, n))
                src = raw[:, c % SLOTS, :].rearrange("p (t k j) -> p k t j", t=NT, j=Q)[:, u * UK:(u + 1) * UK]
                dve.transpose(dst.rearrange("p (k t j) -> p k t j", k=UK, j=Q), src).then_inc(units_turned, 1)

            def make_lo(q, n):
                s, _ = ring_slot(n)
                dve.wait_ge(his_made, q * UP + n + 1)
                dve.tensor_tensor(lo[:, s], turned_v[:, :],
                                  hi[:, s].bitcast(f32), ALU.subtract).then_inc(v_los_made, 1)

            def add_rows(ms):
                dve.tensor_tensor(rows[:, ms], back[:, ms], rows[:, ms], ALU.add).then_inc(sums_made, 1)

            def make_stats(b, m):
                dve.wait_ge(sums_made, b + 1)
                dve.bn_stats(stats[:, m], rows[:, m]).then_inc(stats_made, 1)

            def make_mv(m):
                return dve.bn_aggr(mv[:, m], stats[:, m])

            def make_rstd(b, ms):
                dve.wait_ge(stds_made, b + 1)
                dve.reciprocal(rstd[:, ms], std[:, ms]).then_inc(rstds_made, 1)

            def make_shift(b, ms):
                dve.wait_ge(rstds_made, b + 1)
                dve.scalar_tensor_tensor(out=shift[:, ms], in0=mv[:, ms, 0], scalar=-1.0, in1=rstd[:, ms],
                                         op0=ALU.mult, op1=ALU.mult).then_inc(shifts_made, 1)

            def ending(q, h, u):
                b, whole = q * 2 + h, slice(0, MT)
                if u == 13:
                    dve.wait_ge(relus_turned, (b + 1) * MT)
                    dve.wait_ge(rows_loaded, (b + 1) * 16)
                    add_rows(whole)
                if u == 14:
                    for m in range(MT):
                        make_stats(b, m)
                if u == 15:
                    dve.wait_ge(stats_made, (b + 1) * MT)
                if u == 16:
                    for m in range(MT):
                        last = make_mv(m)
                    last.then_inc(mvs_made, 1)
                if u == 20:
                    make_rstd(b, whole)
                if u == 21:
                    make_shift(b, whole)

            def pair(q):
                for n in range(UP):
                    for g in range(EARLY, GROUPS):
                        if known_met(q) and n == late(g, STEP):
                            make_step(g)
                    if not (known_met(q) and n < TURNED):
                        turn(q, n)
                    if n and kinds[n - 1] == "V" and not (known_met(q) and n < TURNED):
                        make_lo(q, n - 1)
                    if n < UB and not known_met(q):
                        ending(q - 1, 1, n)
                    if n >= UB:
                        ending(q, 0, n - UB)

            make_step(0)
            for g in range(1, EARLY):
                if g == EARLY - XK // GK:
                    copy_early_step(g - 1)
                    for n in range(TURNED):
                        turn(0, n)
                    for n in range(TURNED - 1):
                        if kinds[n] == "V":
                            make_lo(0, n)
                make_step(g)
                if g != EARLY - XK // GK:
                    copy_early_step(g - 1)
            copy_early_step(EARLY - 1)
            assert kinds[-1] == "P"
            pair(0)
            with dve.Fori(1, PAIRS) as q:
                pair(q)
            dve.wait_ge(rows_loaded, NBLK * 16)
            for b, ms in PIECES:
                dve.wait_ge(relus_turned, (NBLK - 1) * MT + ms[-1] + 1)
                add_rows(slice(ms[0], ms[-1] + 1))
                for m in ms:
                    make_stats(b, m)
                dve.wait_ge(stats_made, (NBLK - 1) * MT + ms[-1] + 1)
                for m in ms:
                    last = make_mv(m)
                last.then_inc(mvs_made, 1)
            b, ms = PIECES[0]
            make_rstd(b, slice(ms[0], ms[-1] + 1))
            make_shift(b, slice(ms[0], ms[-1] + 1))
            b, ms = PIECES[1]
            make_rstd(b, slice(ms[0], ms[-1] + 1))
            dve.wait_ge(rstds_made, b + 1)
            for m in ms:
                last = dve.tensor_scalar(rows[:, m], rows[:, m], mv[:, m, 0:1], rstd[:, m:m + 1],
                                         ALU.subtract, ALU.mult)
            last.then_inc(last_piece_done, 1)

        @block.tensor
        def _(pe):
            pe.wait_ge(idents_made, 3)
            pe.wait_ge(signs_made, 1)
            for a in range(DH):
                for i in range(DH):
                    last = pe.transpose(ps_wT[:, i, a * P:(a + 1) * P], sign_w[:, a, i * P:(i + 1) * P], ident_b[:])
            last.then_inc(signs_turned, 1)

            def wait_step_copied(n):
                if n < EARLY:
                    pe.wait_ge(early_steps_copied, n + 1)
                else:
                    pe.wait_ge(late_steps_copied, n + 1 - EARLY)

            def turn_step(n):
                pe.wait_ge(steps_made, n + 1)
                if n >= 2:
                    wait_step_copied(n - 2)
                for k in range(GK):
                    for i in range(DH):
                        last = pe.transpose(ps_xT[n % 2][:, k, i], step_x[:, n % STEP_BUFS, k, i * P:(i + 1) * P],
                                            ident_b[:])
                last.then_inc(steps_turned, 1)

            def make_xw(n):
                wait_step_copied(n)
                if n >= 2:
                    pe.wait_ge(xw_copied, max(m for m in range(n) if xw_buf[m] == xw_buf[n]) + 1)
                for k in range(GK):
                    for i in range(DH):
                        last = pe.matmul(ps_xw[xw_buf[n]][:, k], step_xT[:, n % 2, k, i], sign_wT[:, i],
                                         start=(i == 0), stop=(i == DH - 1))
                last.then_inc(xw_made, 1)

            turn_step(0)
            pe.wait_ge(signs_copied, 1)
            for g in range(1, EARLY):
                if g == EARLY - XK // GK:
                    make_xw(g - 1)
                turn_step(g)
                if g != EARLY - XK // GK:
                    make_xw(g - 1)
            make_xw(EARLY - 1)

            def use_unit(q, n):
                h, u = n // UB, n % UB
                s, _ = ring_slot(n)
                if known_met(q) and n == 0:
                    pe.wait_ge(xw_copied, EARLY)
                if known_met(q) and n < UB and n % UPG == 0 and n // UPG >= EARLY:
                    pe.wait_ge(xw_copied, n // UPG + 1)
                if u == 0 and not known_met(q):
                    pe.wait_ge(relus_made, ((q - 1) * 2 + h + 1) * DH)
                pe.wait_ge(p_los_made if kinds[n] == "P" else v_los_made, ordinal(q, n) + 1)

                def product(k, a, part):
                    step = u * UK + k
                    return pe.matmul(acc[h][a], xw[:, step, a * P:(a + 1) * P], part[:, s, k * MB:(k + 1) * MB],
                                     start=(step == 0 and part is hi), stop=(step == CH * KB - 1 and part is lo))

                if u == UB - 1:
                    for a in range(DH):
                        for k in range(UK):
                            for part in (hi, lo):
                                last = product(k, a, part)
                        if a == 0:
                            last.then_inc(first_halves, 1)
                else:
                    for k in range(UK):
                        for a in range(DH):
                            for part in (hi, lo):
                                last = product(k, a, part)
                last.then_inc(units_used, 1)

            def turn_back(q, h):
                if not known_met(q * 2 + h):
                    pe.wait_ge(sums_made, q * 2 + h)
                for a in range(DH):
                    pe.wait_ge(relus_made, (q * 2 + h) * DH + a + 1)
                    for m in range(MT):
                        last = pe.transpose(back[:, m, a * P:(a + 1) * P], relu[:, a, m * P:(m + 1) * P],
                                            ident[:])
                        if a == DH - 1:
                            last.then_inc(relus_turned, 1)

            BACK_AT = 4

            def pair(q):
                for n in range(UP):
                    for g in range(EARLY, GROUPS):
                        if known_met(q) and n == late(g, TURN):
                            turn_step(g)
                        if known_met(q) and n == late(g, XW):
                            make_xw(g)
                    use_unit(q, n)
                    if n == BACK_AT and not known_met(q):
                        turn_back(q - 1, 1)
                    if n == UB + BACK_AT:
                        turn_back(q, 0)

            pair(0)
            with pe.Fori(1, PAIRS) as q:
                pair(q)
            turn_back(PAIRS - 1, 1)


_INS = ['x', 'adj', 'L0_gnn_weight']
_OUTS = [((8192, 256), 'float32')]


def kernel(**inputs):
    import numpy as _np
    import concourse.bacc as _bacc
    from concourse import mybir as _mybir
    from concourse.bass_utils import run_bass_kernel_spmd as _run

    nc = _bacc.Bacc("TRN2", target_bir_lowering=False, num_devices=1)
    arrays, args = {}, []
    for name in _INS:
        a = _np.ascontiguousarray(inputs[name])
        arrays[f"in_{name}_dram"] = a
        args.append(nc.dram_tensor(f"in_{name}_dram", a.shape, _mybir.dt.from_np(a.dtype), kind="ExternalInput").ap())
    for i, (shape, dtype) in enumerate(_OUTS):
        dt = _mybir.dt.from_np(_np.dtype(dtype))
        args.append(nc.dram_tensor(f"out_{i}_dram", shape, dt, kind="ExternalOutput").ap())
    build(nc, *args)
    r = _run(nc, [arrays], core_ids=[0])
    got = tuple(r.results[0][f"out_{i}_dram"] for i in range(len(_OUTS)))
    return got[0]
```
